# Optimizing a Trainium2 kernel written in Bass

```python
import numpy as np
import jax
import jax.numpy as jnp

def _softmax(x, axis=-1):
    return jax.nn.softmax(x, axis=axis)

def _gelu(x):
    return jax.nn.gelu(x, approximate=True)

def _silu(x):
    return jax.nn.silu(x)

def _sigmoid(x):
    return jax.nn.sigmoid(x)

def _layernorm(x, axis=-1, eps=1e-05):
    m = jnp.mean(x, axis=axis, keepdims=True)
    v = jnp.var(x, axis=axis, keepdims=True)
    return (x - m) / jnp.sqrt(v + eps)

def _scatter_add(tgt, idx, src, axis=0):
    return tgt.at[idx].add(src)

def _segment_sum(src, seg, n):
    return jax.ops.segment_sum(src, seg, n)
kernel_name = 'mk_xattn_seq_d4_seqx_r8_344c4d'

def setup_inputs(seed: int=0):
    np.random.seed(seed)
    _w = jnp.asarray

    def _rec_inputs():
        import jax
        import jax.numpy as jnp
        _rk = jax.random.key(seed)
        x = -0.000125 + 0.9999 * jax.random.normal(jax.random.fold_in(_rk, 1), (128, 64, 128), jnp.float32)
        _lenS = 64 - jax.random.randint(jax.random.fold_in(_rk, 7), (128,), 0, max(1, 64 // 4) + 1, jnp.int32)
        _lenS2 = 64 - jax.random.randint(jax.random.fold_in(_rk, 8), (128,), 0, max(1, 64 // 4) + 1, jnp.int32)
        _ctx_2048P = jax.random.normal(jax.random.fold_in(_rk, 11), (128, 16, 256), jnp.float32)
        _ctx_2048c = jax.random.dirichlet(jax.random.fold_in(_rk, 511), 0.3 * jnp.ones((16,), jnp.float32), (128, 64))
        _ctx_2048t = jnp.einsum('bsk,bkd->bsd', _ctx_2048c, _ctx_2048P)
        _ctx_2048t = _ctx_2048t * jax.lax.rsqrt(jnp.mean(jnp.square(_ctx_2048t)) + 1e-12) * 0.953939
        ctx_2048 = 5.36139e-06 + 1.00015 * (_ctx_2048t + 0.3 * jax.random.normal(jax.random.fold_in(_rk, 611), (128, 64, 256), jnp.float32))
        _validS = jnp.arange(64)[None, :] < _lenS[:, None]
        _validS2 = jnp.arange(64)[None, :] < _lenS2[:, None]
        _causal = jnp.tril(jnp.ones((64, 64), dtype=bool))
        mask_S_fk1 = jnp.where(_validS[0], 1.0, 0.0).astype(jnp.float32)
        mask_S_fk0 = jnp.where(_validS[0], 0.0, 1.0).astype(jnp.float32)
        return (x, ctx_2048, mask_S_fk1, mask_S_fk0)
    x, ctx_2048, mask_S_fk1, mask_S_fk0 = _rec_inputs()

    def _L0_xattn_setup():
        import jax, jax.numpy as jnp
        import numpy as np
        HEADS = 16
        HEAD_DIM = 64
        SUPPRESS = 20.0
        key = jax.random.key(seed)
        ks = jax.random.split(key, 8)
        B, HW, C, T, CT = (8, 512, 128, 77, 256)
        inner = HEADS * HEAD_DIM
        scale = 0.02
        return {'hidden_states': jax.random.normal(ks[0], (B, HW, C), jnp.float32), 'encoder_hidden_states': jax.random.normal(ks[1], (B, T, CT), jnp.float32), 'mask_A': (jax.random.uniform(ks[2], (HW,)) > 0.5).astype(jnp.float32), 'mask_B': (jax.random.uniform(ks[3], (HW,)) > 0.5).astype(jnp.float32), 'Wq': jax.random.normal(ks[4], (C, inner), jnp.float32) * scale, 'Wk': jax.random.normal(ks[5], (CT, inner), jnp.float32) * scale, 'Wv': jax.random.normal(ks[6], (CT, inner), jnp.float32) * scale, 'Wo': jax.random.normal(ks[7], (inner, C), jnp.float32) * scale, 'bo': jnp.zeros((C,), jnp.float32), 'token_indices_A': jnp.array([2, 3], dtype=jnp.int64), 'token_indices_B': jnp.array([5, 6], dtype=jnp.int64)}
    _L0_xattn_all = _L0_xattn_setup()
    _L0_xattn_in = {k: v for k, v in _L0_xattn_all.items() if k in ('Wq', 'Wk', 'Wv', 'Wo', 'bo', 'token_indices_A', 'token_indices_B')}
    del _L0_xattn_all

    def _L1_xattn_setup():
        import jax, jax.numpy as jnp
        import numpy as np
        D_MODEL = 128
        N_HEADS = 16
        N_KV_HEADS = 4
        HEAD_DIM = D_MODEL // N_HEADS
        SPEAKER_DIM = 256
        EPS = 1e-05

        def rmsnorm(x, w, eps=EPS):
            xf = x.astype(jnp.float32)
            inv = jax.lax.rsqrt(jnp.mean(xf * xf, axis=-1, keepdims=True) + eps)
            return (xf * inv).astype(x.dtype) * w
        key = jax.random.key(seed)
        ks = jax.random.split(key, 7)
        B, T, S = (4, 256, 64)
        x = jax.random.normal(ks[0], (B, T, D_MODEL), dtype=jnp.float32)
        cond = jax.random.normal(ks[1], (B, S, SPEAKER_DIM), dtype=jnp.float32)
        sq = 0.02
        wq = jax.random.normal(ks[2], (D_MODEL, N_HEADS * HEAD_DIM), dtype=jnp.float32) * sq
        wk = jax.random.normal(ks[3], (SPEAKER_DIM, N_KV_HEADS * HEAD_DIM), dtype=jnp.float32) * sq
        wv = jax.random.normal(ks[4], (SPEAKER_DIM, N_KV_HEADS * HEAD_DIM), dtype=jnp.float32) * sq
        wo = jax.random.normal(ks[5], (N_HEADS * HEAD_DIM, D_MODEL), dtype=jnp.float32) * sq
        norm_w = jnp.ones((D_MODEL,), dtype=jnp.float32)
        return {'x': x, 'cond': cond, 'wq': wq, 'wk': wk, 'wv': wv, 'wo': wo, 'norm_w': norm_w}
    _L1_xattn_all = _L1_xattn_setup()
    _L1_xattn_in = {k: v for k, v in _L1_xattn_all.items() if k in ('wq', 'wk', 'wv', 'wo', 'norm_w')}
    del _L1_xattn_all

    def _L2_xattn_setup():
        import jax, jax.numpy as jnp
        import numpy as np
        D_MODEL = 128
        N_HEADS = 16
        N_KV_HEADS = 4
        HEAD_DIM = D_MODEL // N_HEADS
        SPEAKER_DIM = 256
        EPS = 1e-05

        def rmsnorm(x, w, eps=EPS):
            xf = x.astype(jnp.float32)
            inv = jax.lax.rsqrt(jnp.mean(xf * xf, axis=-1, keepdims=True) + eps)
            return (xf * inv).astype(x.dtype) * w
        key = jax.random.key(seed)
        ks = jax.random.split(key, 7)
        B, T, S = (4, 256, 64)
        x = jax.random.normal(ks[0], (B, T, D_MODEL), dtype=jnp.float32)
        cond = jax.random.normal(ks[1], (B, S, SPEAKER_DIM), dtype=jnp.float32)
        sq = 0.02
        wq = jax.random.normal(ks[2], (D_MODEL, N_HEADS * HEAD_DIM), dtype=jnp.float32) * sq
        wk = jax.random.normal(ks[3], (SPEAKER_DIM, N_KV_HEADS * HEAD_DIM), dtype=jnp.float32) * sq
        wv = jax.random.normal(ks[4], (SPEAKER_DIM, N_KV_HEADS * HEAD_DIM), dtype=jnp.float32) * sq
        wo = jax.random.normal(ks[5], (N_HEADS * HEAD_DIM, D_MODEL), dtype=jnp.float32) * sq
        norm_w = jnp.ones((D_MODEL,), dtype=jnp.float32)
        return {'x': x, 'cond': cond, 'wq': wq, 'wk': wk, 'wv': wv, 'wo': wo, 'norm_w': norm_w}
    _L2_xattn_all = _L2_xattn_setup()
    _L2_xattn_in = {k: v for k, v in _L2_xattn_all.items() if k in ('wq', 'wk', 'wv', 'wo', 'norm_w')}
    del _L2_xattn_all

    def _L3_xattn_setup():
        import jax, jax.numpy as jnp
        import numpy as np
        D_MODEL = 128
        N_HEADS = 16
        N_KV_HEADS = 4
        HEAD_DIM = D_MODEL // N_HEADS
        SPEAKER_DIM = 256
        EPS = 1e-05

        def rmsnorm(x, w, eps=EPS):
            xf = x.astype(jnp.float32)
            inv = jax.lax.rsqrt(jnp.mean(xf * xf, axis=-1, keepdims=True) + eps)
            return (xf * inv).astype(x.dtype) * w
        key = jax.random.key(seed)
        ks = jax.random.split(key, 7)
        B, T, S = (4, 256, 64)
        x = jax.random.normal(ks[0], (B, T, D_MODEL), dtype=jnp.float32)
        cond = jax.random.normal(ks[1], (B, S, SPEAKER_DIM), dtype=jnp.float32)
        sq = 0.02
        wq = jax.random.normal(ks[2], (D_MODEL, N_HEADS * HEAD_DIM), dtype=jnp.float32) * sq
        wk = jax.random.normal(ks[3], (SPEAKER_DIM, N_KV_HEADS * HEAD_DIM), dtype=jnp.float32) * sq
        wv = jax.random.normal(ks[4], (SPEAKER_DIM, N_KV_HEADS * HEAD_DIM), dtype=jnp.float32) * sq
        wo = jax.random.normal(ks[5], (N_HEADS * HEAD_DIM, D_MODEL), dtype=jnp.float32) * sq
        norm_w = jnp.ones((D_MODEL,), dtype=jnp.float32)
        return {'x': x, 'cond': cond, 'wq': wq, 'wk': wk, 'wv': wv, 'wo': wo, 'norm_w': norm_w}
    _L3_xattn_all = _L3_xattn_setup()
    _L3_xattn_in = {k: v for k, v in _L3_xattn_all.items() if k in ('wq', 'wk', 'wv', 'wo', 'norm_w')}
    del _L3_xattn_all
    return {'x': x, 'ctx_2048': ctx_2048, 'mask_S_fk1': mask_S_fk1, 'mask_S_fk0': mask_S_fk0, 'L0_xattn_Wq': _L0_xattn_in['Wq'], 'L0_xattn_Wk': _L0_xattn_in['Wk'], 'L0_xattn_Wv': _L0_xattn_in['Wv'], 'L0_xattn_Wo': _L0_xattn_in['Wo'], 'L0_xattn_bo': _L0_xattn_in['bo'], 'L0_xattn_token_indices_A': _L0_xattn_in['token_indices_A'], 'L0_xattn_token_indices_B': _L0_xattn_in['token_indices_B'], 'L1_xattn_wq': _L1_xattn_in['wq'], 'L1_xattn_wk': _L1_xattn_in['wk'], 'L1_xattn_wv': _L1_xattn_in['wv'], 'L1_xattn_wo': _L1_xattn_in['wo'], 'L1_xattn_norm_w': _L1_xattn_in['norm_w'], 'L2_xattn_wq': _L2_xattn_in['wq'], 'L2_xattn_wk': _L2_xattn_in['wk'], 'L2_xattn_wv': _L2_xattn_in['wv'], 'L2_xattn_wo': _L2_xattn_in['wo'], 'L2_xattn_norm_w': _L2_xattn_in['norm_w'], 'L3_xattn_wq': _L3_xattn_in['wq'], 'L3_xattn_wk': _L3_xattn_in['wk'], 'L3_xattn_wv': _L3_xattn_in['wv'], 'L3_xattn_wo': _L3_xattn_in['wo'], 'L3_xattn_norm_w': _L3_xattn_in['norm_w']}

def reference(x, ctx_2048, mask_S_fk1, mask_S_fk0, L0_xattn_Wq, L0_xattn_Wk, L0_xattn_Wv, L0_xattn_Wo, L0_xattn_bo, L0_xattn_token_indices_A, L0_xattn_token_indices_B, L1_xattn_wq, L1_xattn_wk, L1_xattn_wv, L1_xattn_wo, L1_xattn_norm_w, L2_xattn_wq, L2_xattn_wk, L2_xattn_wv, L2_xattn_wo, L2_xattn_norm_w, L3_xattn_wq, L3_xattn_wk, L3_xattn_wv, L3_xattn_wo, L3_xattn_norm_w):
    import jax
    import jax.numpy as jnp

    def _L0_xattn_ref(hidden_states, encoder_hidden_states, mask_A, mask_B, Wq, Wk, Wv, Wo, bo, token_indices_A, token_indices_B):
        import jax, jax.numpy as jnp
        import numpy as np
        HEADS = 16
        HEAD_DIM = 64
        SUPPRESS = 20.0
        B, HW, C = hidden_states.shape
        T = encoder_hidden_states.shape[1]
        residual = hidden_states
        q = hidden_states @ Wq
        k = encoder_hidden_states @ Wk
        v = encoder_hidden_states @ Wv
        q = q.reshape(B, HW, HEADS, HEAD_DIM).transpose(0, 2, 1, 3)
        k = k.reshape(B, T, HEADS, HEAD_DIM).transpose(0, 2, 1, 3)
        v = v.reshape(B, T, HEADS, HEAD_DIM).transpose(0, 2, 1, 3)
        scale = HEAD_DIM ** (-0.5)
        logits = jnp.einsum('bhqd,bhkd->bhqk', q, k) * scale
        suppress_A_in = 1.0 - mask_A
        suppress_B_in = 1.0 - mask_B
        col_bias = jnp.zeros((HW, T), logits.dtype)
        col_bias = col_bias.at[:, token_indices_A].set((-SUPPRESS * suppress_A_in)[:, None])
        col_bias = col_bias.at[:, token_indices_B].set((-SUPPRESS * suppress_B_in)[:, None])
        logits = logits + col_bias[None, None, :, :]
        probs = jax.nn.softmax(logits, axis=-1)
        out = jnp.einsum('bhqk,bhkd->bhqd', probs, v)
        out = out.transpose(0, 2, 1, 3).reshape(B, HW, HEADS * HEAD_DIM)
        out = out @ Wo + bo
        out = out + residual
        return out

    def _L1_xattn_ref(x, cond, wq, wk, wv, wo, norm_w):
        import jax, jax.numpy as jnp
        import numpy as np
        D_MODEL = 128
        N_HEADS = 16
        N_KV_HEADS = 4
        HEAD_DIM = D_MODEL // N_HEADS
        SPEAKER_DIM = 256
        EPS = 1e-05

        def rmsnorm(x, w, eps=EPS):
            xf = x.astype(jnp.float32)
            inv = jax.lax.rsqrt(jnp.mean(xf * xf, axis=-1, keepdims=True) + eps)
            return (xf * inv).astype(x.dtype) * w
        B, T, _ = x.shape
        S = cond.shape[1]
        n_rep = N_HEADS // N_KV_HEADS
        residual = x
        xn = rmsnorm(x, norm_w)
        q = (xn @ wq).reshape(B, T, N_HEADS, HEAD_DIM)
        k = (cond @ wk).reshape(B, S, N_KV_HEADS, HEAD_DIM)
        v = (cond @ wv).reshape(B, S, N_KV_HEADS, HEAD_DIM)
        qg = q.reshape(B, T, N_KV_HEADS, n_rep, HEAD_DIM)
        scale = 1.0 / np.sqrt(HEAD_DIM).astype(np.float32)
        scores = jnp.einsum('btgrd,bsgd->bgrts', qg, k) * scale
        attn = jax.nn.softmax(scores.astype(jnp.float32), axis=-1).astype(q.dtype)
        out = jnp.einsum('bgrts,bsgd->btgrd', attn, v).reshape(B, T, N_HEADS * HEAD_DIM)
        return residual + out @ wo

    def _L2_xattn_ref(x, cond, wq, wk, wv, wo, norm_w):
        import jax, jax.numpy as jnp
        import numpy as np
        D_MODEL = 128
        N_HEADS = 16
        N_KV_HEADS = 4
        HEAD_DIM = D_MODEL // N_HEADS
        SPEAKER_DIM = 256
        EPS = 1e-05

        def rmsnorm(x, w, eps=EPS):
            xf = x.astype(jnp.float32)
            inv = jax.lax.rsqrt(jnp.mean(xf * xf, axis=-1, keepdims=True) + eps)
            return (xf * inv).astype(x.dtype) * w
        B, T, _ = x.shape
        S = cond.shape[1]
        n_rep = N_HEADS // N_KV_HEADS
        residual = x
        xn = rmsnorm(x, norm_w)
        q = (xn @ wq).reshape(B, T, N_HEADS, HEAD_DIM)
        k = (cond @ wk).reshape(B, S, N_KV_HEADS, HEAD_DIM)
        v = (cond @ wv).reshape(B, S, N_KV_HEADS, HEAD_DIM)
        qg = q.reshape(B, T, N_KV_HEADS, n_rep, HEAD_DIM)
        scale = 1.0 / np.sqrt(HEAD_DIM).astype(np.float32)
        scores = jnp.einsum('btgrd,bsgd->bgrts', qg, k) * scale
        attn = jax.nn.softmax(scores.astype(jnp.float32), axis=-1).astype(q.dtype)
        out = jnp.einsum('bgrts,bsgd->btgrd', attn, v).reshape(B, T, N_HEADS * HEAD_DIM)
        return residual + out @ wo

    def _L3_xattn_ref(x, cond, wq, wk, wv, wo, norm_w):
        import jax, jax.numpy as jnp
        import numpy as np
        D_MODEL = 128
        N_HEADS = 16
        N_KV_HEADS = 4
        HEAD_DIM = D_MODEL // N_HEADS
        SPEAKER_DIM = 256
        EPS = 1e-05

        def rmsnorm(x, w, eps=EPS):
            xf = x.astype(jnp.float32)
            inv = jax.lax.rsqrt(jnp.mean(xf * xf, axis=-1, keepdims=True) + eps)
            return (xf * inv).astype(x.dtype) * w
        B, T, _ = x.shape
        S = cond.shape[1]
        n_rep = N_HEADS // N_KV_HEADS
        residual = x
        xn = rmsnorm(x, norm_w)
        q = (xn @ wq).reshape(B, T, N_HEADS, HEAD_DIM)
        k = (cond @ wk).reshape(B, S, N_KV_HEADS, HEAD_DIM)
        v = (cond @ wv).reshape(B, S, N_KV_HEADS, HEAD_DIM)
        qg = q.reshape(B, T, N_KV_HEADS, n_rep, HEAD_DIM)
        scale = 1.0 / np.sqrt(HEAD_DIM).astype(np.float32)
        scores = jnp.einsum('btgrd,bsgd->bgrts', qg, k) * scale
        attn = jax.nn.softmax(scores.astype(jnp.float32), axis=-1).astype(q.dtype)
        out = jnp.einsum('bgrts,bsgd->btgrd', attn, v).reshape(B, T, N_HEADS * HEAD_DIM)
        return residual + out @ wo
    x = _L0_xattn_ref(x, ctx_2048, mask_S_fk1, mask_S_fk0, L0_xattn_Wq, L0_xattn_Wk, L0_xattn_Wv, L0_xattn_Wo, L0_xattn_bo, L0_xattn_token_indices_A, L0_xattn_token_indices_B)
    x = _L1_xattn_ref(x, ctx_2048, L1_xattn_wq, L1_xattn_wk, L1_xattn_wv, L1_xattn_wo, L1_xattn_norm_w)
    x = _L2_xattn_ref(x, ctx_2048, L2_xattn_wq, L2_xattn_wk, L2_xattn_wv, L2_xattn_wo, L2_xattn_norm_w)
    x = _L3_xattn_ref(x, ctx_2048, L3_xattn_wq, L3_xattn_wk, L3_xattn_wv, L3_xattn_wo, L3_xattn_norm_w)
    return x

_drawn_inputs = setup_inputs


def setup_inputs(seed=0):
    import zlib

    import numpy as np

    out = dict(_drawn_inputs(seed))
    spreads = {'L0_xattn_bo': (0.0, 0.1),
     'L1_xattn_norm_w': (1.0, 0.6),
     'L2_xattn_norm_w': (1.0, 0.6),
     'L3_xattn_norm_w': (1.0, 0.6)}
    factors = {'mask_S_fk1': 8.0,
     'mask_S_fk0': 8.0,
     'L0_xattn_Wq': 8.0,
     'L0_xattn_Wk': 8.0,
     'L1_xattn_wq': 8.0,
     'L1_xattn_wk': 8.0,
     'L2_xattn_wq': 8.0,
     'L2_xattn_wk': 8.0,
     'L3_xattn_wq': 8.0,
     'L3_xattn_wk': 8.0}
    for name, (base, spread) in spreads.items():
        noise = np.random.default_rng([zlib.crc32(name.encode()), seed]).standard_normal(out[name].shape)
        drawn = base * np.exp(spread * noise) if base else spread * noise
        out[name] = jnp.asarray(drawn.astype(out[name].dtype))
    for name, factor in factors.items():
        out[name] = (out[name] * factor).astype(out[name].dtype)
    return out
```

```python
from contextlib import ExitStack

import numpy as np

import concourse.bass as bass
from concourse import mybir

ALU = mybir.AluOpType
ACT = mybir.ActivationFunctionType
F32 = mybir.dt.float32
BF16 = mybir.dt.bfloat16
I32 = mybir.dt.int32
AX = mybir.AxisListType.X

B, S, C, CT = 128, 64, 128, 256
G = 4
T = G * S
NG = B // G
NS = 3
NP = G // 2
EPS = 1e-5
SCALE8 = float(np.float32(1.0) / np.sqrt(8).astype(np.float32))
PE, AC, DV, PO, SP = "tensor", "scalar", "vector", "gpsimd", "sync"


class Queues:

    def __init__(self, ctx, nc):
        self.ctx, self.nc = ctx, nc
        self.todo = {e: [] for e in (PE, AC, DV, PO, SP)}
        self.seen = {e: {} for e in self.todo}
        self.sems, self.count = {}, {}

    def op(self, eng, fn, wait=(), sig=None, inc=1):
        for name, value in wait:
            if self.seen[eng].get(name, 0) < value:
                self.seen[eng][name] = value
                self.todo[eng].append(lambda e, s=self.sems[name], v=value: e.wait_ge(s, v))
        if sig is None:
            self.todo[eng].append(fn)
            return None
        if sig not in self.sems:
            self.sems[sig] = self.ctx.enter_context(self.nc.semaphore(sig))
            self.count[sig] = 0
        self.count[sig] += inc
        self.todo[eng].append(lambda e, s=self.sems[sig]: fn(e).then_inc(s, inc))
        return (sig, self.count[sig])

    def dma(self, eng, out, in_, sig, wait=()):
        return self.op(eng, lambda e: e.dma_start(out, in_), wait, sig, 16)

    def play(self, eng, e):
        for step in self.todo[eng]:
            step(e)


class Ring:

    def __init__(self, bufs):
        self.bufs, self.free = bufs, [(i, []) for i in range(len(bufs))]

    def take(self):
        i, waits = self.free.pop(0)
        return i, self.bufs[i], waits

    def release(self, i, *tokens):
        self.free.append((i, list(tokens)))


def xattn_kernel(nc, t):
    with ExitStack() as ctx:
        def sb(name, shape, dt=F32):
            return ctx.enter_context(nc.sbuf_tensor(name, shape, dt))

        q = Queues(ctx, nc)
        op = q.op
        banks = [ctx.enter_context(nc.psum_tensor(f"bank{i}", [128, 512], F32)) for i in range(8)]
        rS, rT, rP = Ring(banks[0:3]), Ring(banks[3:5]), Ring(banks[5:8])
        rE = Ring([sb(f"E{i}", [128, 512]) for i in range(12)])
        rV = Ring([sb(f"st{i}", [128, 24]) for i in range(12)])

        ident = sb("ident", [128, 128])
        mean = sb("mean", [128, 128])
        rmask = sb("rmask", [128, 6])
        wq0 = sb("wq0", [128, 1024])
        wk0 = sb("wk0", [128, 2, 1024])
        wv0 = sb("wv0", [128, 2, 1024])
        wo0 = sb("wo0", [128, 8, 128])
        bo = sb("bo", [128, 1])
        nw = sb("nw", [128, 3])
        wqs = sb("wqs", [128, 3, 128])
        wkr = sb("wkr", [128, 3, 2, 128])
        wks = sb("wks", [128, 3, 2, 32])
        wvs = sb("wvs", [128, 2, 3, 32])
        wos = sb("wos", [128, 3, 128])
        BV = sb("BV", [128, 128], BF16)
        BI = sb("BI", [128, 512], BF16)

        la = [q.dma(SP, ident[:, :], t["c_ident"], "l_ident"),
              q.dma(SP, rmask[:, :], t["c_rmask"], "l_rmask")]
        l_ident, l_rmask = la
        streams = []
        for s in range(NS):
            streams.append(dict(
                s=s,
                xin=sb(f"xin{s}", [128, NP, C]), cin=sb(f"cin{s}", [128, NP, CT]),
                xT=sb(f"xT{s}", [128, T]), x2=sb(f"x2{s}", [128, T]), cT=sb(f"cT{s}", [128, 2, T]),
                inv=sb(f"inv{s}", [128, NP]), nt=sb(f"nt{s}", [128, 4, NP]),
                QT=sb(f"QT{s}", [128, 8, T]), KT=sb(f"KT{s}", [128, 8, T]),
                V=sb(f"V{s}", [128, G, 512]), V3=sb(f"V3{s}", [128, G, 96]),
                VB=sb(f"VB{s}", [128, G, 4, 2, 32]), ot=sb(f"ot{s}", [128, T]), in_free=[]))

        x_r = t["x"].rearrange("(n p b) s c -> n (b s) p c", p=NP, b=2)
        c_r = t["ctx_2048"].rearrange("(n p b) s c -> n (b s) p c", p=NP, b=2)
        o_r = t["out"].rearrange("(n p b) s c -> n (b s) p c", p=NP, b=2)

        def load_in(st, g):
            s = st["s"]
            st["l_x"] = q.dma(SP, st["xin"][:, :, :], x_r[g], f"l_x{s}", st["in_free"])
            st["l_c"] = q.dma(SP, st["cin"][:, :, :], c_r[g], f"l_c{s}", st["in_free"])

        load_in(streams[0], 0)
        l_wq = q.dma(SP, wq0[:, :], t["L0_xattn_Wq"], "l_wq")
        l_wk = q.dma(SP, wk0[:, :, :], t["L0_xattn_Wk"].rearrange("(k p) n -> p k n", p=128), "l_wk")
        l_wv = q.dma(SP, wv0[:, :, :], t["L0_xattn_Wv"].rearrange("(k p) n -> p k n", p=128), "l_wv")
        for l in range(3):
            n = f"L{l + 1}_xattn_"
            q.dma(SP, wqs[:, l, :], t[n + "wq"], "l_sm")
            q.dma(SP, wks[:, l, :, :], t[n + "wk"].rearrange("(k p) n -> p k n", p=128), "l_sm")
            q.dma(SP, wvs[:, :, l, :], t[n + "wv"].rearrange("(k p) n -> p k n", p=128), "l_sm")
            q.dma(SP, wos[:, l, :], t[n + "wo"], "l_sm")
            q.dma(SP, nw[:, l:l + 1], t[n + "norm_w"].rearrange("(c a) -> c a", a=1), "l_sm")
        q.dma(SP, bo[:, :], t["L0_xattn_bo"].rearrange("(c a) -> c a", a=1), "l_sm")
        q.dma(SP, mean[:, :], t["c_mean"], "l_sm")
        l_sm = q.dma(SP, wo0[:, :, :], t["L0_xattn_Wo"].rearrange("(j p) n -> p j n", p=128), "l_sm")
        for s in range(1, NS):
            load_in(streams[s], s)

        idx = sb("idx", [1, 4], I32)
        idf = sb("idf", [1, 4])
        neg = sb("neg", [1, 4])
        iota = sb("iota", [1, 64])
        mk = sb("mk", [1, 2, 64])
        eq = sb("eq", [1, 4, 64])
        inn = sb("inn", [1, 3, 64])
        vv = sb("vv", [1, 2, 64])
        vb = sb("vb", [1, 3, 2, 64], BF16)
        vrow = sb("vrow", [1, 3, 2, 2, 64], BF16)
        irow = sb("irow", [1, 2, 8, 64], BF16)
        q.dma(SP, idx[:, 0:2], t["L0_xattn_token_indices_A"].rearrange("(a n) -> a n", a=1), "l_b")
        q.dma(SP, idx[:, 2:4], t["L0_xattn_token_indices_B"].rearrange("(a n) -> a n", a=1), "l_b")
        q.dma(SP, iota[:, :], t["c_iota"], "l_b")
        q.dma(SP, mk[:, 0, :], t["mask_S_fk1"].rearrange("(a n) -> a n", a=1), "l_b")
        l_b = q.dma(SP, mk[:, 1, :], t["mask_S_fk0"].rearrange("(a n) -> a n", a=1), "l_b")

        z1 = op(PO, lambda e: e.memset(BV[:, :], 0.0), (), "p_zero")
        z1 = op(PO, lambda e: e.memset(BI[:, :], 0.0), (), "p_zero")
        for st in streams:
            st["z_vb"] = op(PO, lambda e, st=st: e.memset(st["VB"][:, :, :, :, :], 0.0), (), "p_zero")

        chain = [l_b]

        def link(fn):
            chain[0] = op(DV, fn, chain, "d_setup")
            return chain[0]

        link(lambda e: e.tensor_copy(idf[:, :], idx[:, :]))
        link(lambda e: e.tensor_scalar(neg[:, :], idf[:, :], 0.0, 64.0, ALU.is_lt, ALU.mult))
        link(lambda e: e.tensor_tensor(idf[:, :], idf[:, :], neg[:, :], ALU.add))
        for i in range(4):
            link(lambda e, i=i: e.tensor_scalar(eq[:, i, :], iota[:, :], idf[:, i:i + 1], None, ALU.is_equal))
        link(lambda e: e.tensor_tensor(inn[:, 0, :], eq[:, 0, :], eq[:, 1, :], ALU.max))
        link(lambda e: e.tensor_tensor(inn[:, 1, :], eq[:, 2, :], eq[:, 3, :], ALU.max))
        link(lambda e: e.tensor_tensor(inn[:, 2, :], inn[:, 0, :], inn[:, 1, :], ALU.mult))
        link(lambda e: e.tensor_tensor(inn[:, 0, :], inn[:, 0, :], inn[:, 2, :], ALU.subtract))
        for i in range(8):
            link(lambda e, i=i: e.tensor_copy(irow[:, :, i, :], inn[:, 0:2, :]))
        link(lambda e: e.tensor_scalar(mk[:, :, :], mk[:, :, :], -1.0, 1.0, ALU.mult, ALU.add))
        link(lambda e: e.tensor_scalar(vv[:, :, :], mk[:, :, :], -20.0, None, ALU.mult))
        for i in range(3):
            link(lambda e, i=i: e.tensor_copy(vb[:, i, :, :], vv[:, :, :]))
            if i < 2:
                link(lambda e, i=i: e.tensor_tensor(vv[:, :, :], vv[:, :, :], vb[:, i, :, :], ALU.subtract))
        for b in range(2):
            link(lambda e, b=b: e.tensor_copy(vrow[:, :, :, b, :], vb[:, :, :, :]))
        for half in range(2):
            for k in range(2):
                for i in range(3):
                    r = 64 * half + 3 * k + i
                    q.dma(SP, BV[r:r + 1, :], vrow[:, i, k, :, :].rearrange("a b n -> a (b n)"), "l_bias",
                          [chain[0], z1])
                    l_bias = q.dma(SP, BI[r:r + 1, :], irow[:, k, :, :].rearrange("a b n -> a (b n)"), "l_bias",
                                   [chain[0], z1])

        for l in range(3):
            d_w = op(DV, lambda e, l=l: e.tensor_scalar(wqs[:, l, :], wqs[:, l, :], nw[:, l:l + 1], None,
                                                        ALU.mult), [l_sm], "d_w")
            for k in range(2):
                for r in range(4):
                    d_w = op(DV, lambda e, l=l, k=k, r=r: e.tensor_copy(
                        wkr[:, l, k, :].rearrange("p (g r d) -> p g r d", g=4, r=4)[:, :, r, :],
                        wks[:, l, k, :].rearrange("p (g d) -> p g d", g=4)), [l_sm], "d_w")

        turn = [0]

        def evac(fa, fd, wait, sig):
            turn[0] += 1
            if turn[0] % 2:
                return op(AC, fa, wait, "a_" + sig)
            return op(DV, fd, wait, "d_" + sig)

        def copy_out(dst, src, wait, sig):
            return evac(lambda e: e.copy(dst, src), lambda e: e.tensor_copy(dst, src), wait, sig)

        def rsqrt(nt, inv, d):
            v, y, h, w = (nt[:, k, :] for k in range(4))

            def step(fn):
                nonlocal d
                d = op(DV, fn, [d], "d_inv")

            step(lambda e: e.tensor_scalar(h.bitcast(I32), v.bitcast(I32), 1, None, ALU.logical_shift_right))
            step(lambda e: e.tensor_scalar(y.bitcast(I32), h.bitcast(I32), -1.0, float(0x5F3759DF),
                                           ALU.mult, ALU.add))
            for last in (False, True):
                step(lambda e: e.tensor_tensor(w, y, y, ALU.mult))
                step(lambda e: e.tensor_tensor(h, w, v, ALU.mult))
                step(lambda e: e.tensor_scalar(w, h, 0.375, -1.25, ALU.mult, ALU.add))
                step(lambda e: e.tensor_tensor(w, w, h, ALU.mult))
                if last:
                    step(lambda e: e.tensor_scalar(w, w, 1.875, SCALE8, ALU.add, ALU.mult))
                    step(lambda e: e.tensor_tensor(inv[:, :], w, y, ALU.mult))
                else:
                    step(lambda e: e.scalar_tensor_tensor(out=y, in0=w, scalar=1.875, in1=y, op0=ALU.add,
                                                          op1=ALU.mult))
            return d

        def softmax(u, scales, scales_tok, p_s):
            ie, E, efree = rE.take()
            iv, st, vfree = rV.take()
            bank = u["bank"][:, :].rearrange("p (h k) -> p h k", k=64)
            E3 = E[:, :].rearrange("p (h k) -> p h k", k=64)

            def wide(ap):
                return ap.rearrange("p (h a) -> p h a", a=1).to_broadcast([128, 8, 64])

            mx, sm, rc = st[:, 0:8], st[:, 8:16], st[:, 16:24]
            d = op(DV, lambda e: e.tensor_reduce(mx, bank, AX, ALU.max), [p_s, *vfree], "d_max")
            d = op(DV, lambda e: e.tensor_tensor(E3, bank, wide(mx), ALU.subtract), [d, *efree], "d_sub")
            rS.release(u["ibank"], d)
            w = 512 // len(scales)
            for n, sc in enumerate(scales):
                a = op(AC, lambda e, n=n, sc=sc: e.activation(E[:, w * n:w * n + w], E[:, w * n:w * n + w],
                                                              ACT.Exp, scale=sc), [d, *scales_tok], "a_exp")
            d = op(DV, lambda e: e.tensor_reduce(sm, E3, AX, ALU.add), [a], "d_sum")
            r = op(DV, lambda e: e.reciprocal(rc, sm), [d], "d_rcp")
            n = op(PO, lambda e: e.tensor_tensor(E3, E3, wide(rc), ALU.mult), [r], "g_nrm")
            rV.release(iv, n)
            u.update(E=E, iE=ie, tok=n)

        def turned(u):
            it, bank, free = rT.take()
            for k in range(4):
                p = op(PE, lambda e, k=k: e.transpose(bank[:, 128 * k:128 * k + 128],
                                                      u["E"][:, 128 * k:128 * k + 128], ident[:, :]),
                       [u["tok"], *free, l_ident], "p_tr" if k == 3 else None)
            a = op(AC, lambda e: e.copy(u["E"][:, :], bank[:, :]), [p], "a_et")
            rT.release(it, a)
            u.update(ET=u["E"], et=a)

        def group(st, g):
            s = st["s"]
            xT, cT, QT, KT, V, V3, VB = (st[k] for k in ("xT", "cT", "QT", "KT", "V", "V3", "VB"))
            i, bank, free = rP.take()
            for p in range(NP):
                m = op(PE, lambda e, p=p, bank=bank: e.transpose(bank[:, 128 * p:128 * p + 128],
                                                                 st["xin"][:, p, :], ident[:, :]),
                       [st["l_x"], l_ident, *free], "p_io" if p == NP - 1 else None)
            t_x = copy_out(xT[:, :], bank[:, 0:T], [m, *st.get("xT_free", [])], "xT")
            rP.release(i, t_x)
            i, bank, free = rP.take()
            for k in range(2):
                for p in range(NP):
                    m = op(PE, lambda e, p=p, k=k, bank=bank: e.transpose(
                        bank[:, T * k + 128 * p:T * k + 128 * p + 128],
                        st["cin"][:, p, 128 * k:128 * k + 128], ident[:, :]),
                        [st["l_c"], *free], "p_io" if k == 1 and p == NP - 1 else None)
            t_c = copy_out(cT[:, :, :].rearrange("p k n -> p (k n)"), bank[:, :], [m], "cT")
            rP.release(i, t_c)
            st["in_free"] = [m]
            if g + NS < NG:
                load_in(st, g + NS)
            yield
            for half in range(4):
                i, bank, free = rP.take()
                for jj in range(2):
                    j = 2 * half + jj
                    m = op(PE, lambda e, j=j, jj=jj, bank=bank: e.matmul(
                        bank[:, T * jj:T * jj + T], wq0[:, 128 * j:128 * j + 128], xT[:, :],
                        start=True, stop=True), [t_x, l_wq, *free], "p_q" if jj else None)
                dst = QT[:, 2 * half:2 * half + 2, :].rearrange("p j n -> p (j n)")
                t_q = op(AC, lambda e, dst=dst, bank=bank: e.mul(dst, bank[:, :], 0.125), [m], "a_q")
                rP.release(i, t_q)
                i, bank, free = rP.take()
                for jj in range(2):
                    j = 2 * half + jj
                    for k in range(2):
                        m = op(PE, lambda e, j=j, jj=jj, k=k, bank=bank: e.matmul(
                            bank[:, T * jj:T * jj + T], wk0[:, k, 128 * j:128 * j + 128], cT[:, k, :],
                            start=(k == 0), stop=(k == 1)), [t_c, l_wk, *free], "p_k" if jj and k else None)
                dst = KT[:, 2 * half:2 * half + 2, :].rearrange("p j n -> p (j n)")
                t_k = op(DV, lambda e, dst=dst, bank=bank: e.tensor_copy(dst, bank[:, :]), [m], "d_k")
                rP.release(i, t_k)
                yield

            def values(b):
                i, bank, free = rP.take()
                for v in range(2):
                    for k in range(2):
                        m = op(PE, lambda e, v=v, k=k, b=b, bank=bank: e.matmul(
                            bank[64 * v:64 * v + 64, :], cT[:, k, 64 * b:64 * b + 64],
                            wv0[:, k, :].rearrange("p (a v n) -> p a v n", a=4, v=2)[:, :, v, :],
                            start=(k == 0), stop=(k == 1)), [t_c, l_wv, *free], "p_v" if v and k else None)
                r = copy_out(V[:, b, :], bank[:, :], [m], "v")
                rP.release(i, r)
                return r

            def scores0(pair, h2):
                ib, bank, free = rS.take()
                lo = 64 * h2
                for b2 in range(2):
                    op(PE, lambda e, b2=b2: e.matmul(bank[64 * b2:64 * b2 + 64, :],
                                                     BV[lo:lo + 64, 64 * b2:64 * b2 + 64], BI[lo:lo + 64, :],
                                                     start=True, stop=False, skip_group_check=True),
                       [l_bias, *free])
                for j in range(8):
                    for b2 in range(2):
                        n = 128 * pair + 64 * b2
                        m = op(PE, lambda e, j=j, b2=b2, n=n: e.matmul(
                            bank[64 * b2:64 * b2 + 64, 64 * j:64 * j + 64], QT[lo:lo + 64, j, n:n + 64],
                            KT[lo:lo + 64, j, n:n + 64], start=False, stop=True, skip_group_check=True),
                            [t_q, t_k], "p_s" if j == 7 and b2 else None)
                u = dict(bank=bank, ibank=ib)
                softmax(u, [1.0], [], m)
                return u

            units = {}
            t_v = []
            for pair in range(NP):
                for h2 in range(2):
                    units[pair, h2] = scores0(pair, h2)
                    t_v.append(values(2 * pair + h2))
                    yield
            i, bank, free = rP.take()
            for b in range(G):
                for v in range(2):
                    for k in range(2):
                        m = op(PE, lambda e, v=v, k=k, b=b, bank=bank: e.matmul(
                            bank[64 * v:64 * v + 64, 96 * b:96 * b + 96], cT[:, k, 64 * b:64 * b + 64],
                            wvs[:, k, :, :].rearrange("p l n -> p (l n)"), start=(k == 0), stop=(k == 1)),
                            [t_c, l_sm, *free], "p_v" if b == G - 1 and v and k else None)
            t_v3 = copy_out(V3[:, :, :].rearrange("p b n -> p (b n)"), bank[:, 0:96 * G], [m], "v3")
            rP.release(i, t_v3)
            yield
            t_o = []
            for pair in range(NP):
                us = [units[pair, h2] for h2 in range(2)]
                for u in us:
                    turned(u)
                    yield
                for v in range(2):
                    i, bank, free = rP.take()
                    for a in range(4):
                        for b2 in range(2):
                            b = 2 * pair + b2
                            for h2 in range(2):
                                m = op(PE, lambda e, v=v, a=a, b=b, b2=b2, h2=h2, bank=bank, us=us: e.matmul(
                                    bank[64 * h2:64 * h2 + 64, 128 * a + 64 * b2:128 * a + 64 * b2 + 64],
                                    V[64 * v:64 * v + 64, b, 128 * a + 64 * h2:128 * a + 64 * h2 + 64],
                                    us[h2]["ET"][64 * v:64 * v + 64, 128 * a + 64 * b2:128 * a + 64 * b2 + 64],
                                    start=True, stop=True),
                                    [us[h2]["et"], t_v[b], *free], "p_pv" if a == 3 and b2 and h2 else None)
                    dst = QT[:, :, :].rearrange("p (a v) n -> p a v n", v=2)[:, :, v, 128 * pair:128 * pair + 128]
                    r = copy_out(dst, bank[:, :].rearrange("p (a n) -> p a n", a=4), [m], "o")
                    rP.release(i, r)
                    t_o.append(r)
                for u in us:
                    rE.release(u["iE"], m)
                yield
            i, bank, free = rP.take()
            for j in range(8):
                m = op(PE, lambda e, j=j, bank=bank: e.matmul(bank[:, 0:T], wo0[:, j, :], QT[:, j, :],
                                                              start=(j == 0), stop=(j == 7)),
                       [*t_o, l_sm, *free], "p_wo" if j == 7 else None)
            t_x = op(DV, lambda e, bank=bank: e.scalar_tensor_tensor(
                out=xT[:, :], in0=bank[:, 0:T], scalar=bo[:, 0:1], in1=xT[:, :], op0=ALU.add, op1=ALU.add),
                [m], "d_x")
            rP.release(i, t_x)
            yield

            inv, nt, x2, ot = st["inv"], st["nt"], st["x2"], st["ot"]
            KB = KT[:, 0:4, :].rearrange("p j n -> p (j n)").rearrange("p (b r n) -> p b r n", b=G, r=4)
            Q1 = QT[:, 0, :]
            for l in range(3):
                i, bank, free = rP.take()
                for k in range(2):
                    m = op(PE, lambda e, l=l, k=k, bank=bank: e.matmul(
                        bank[:, 0:T], wkr[:, l, k, :], cT[:, k, :], start=(k == 0), stop=(k == 1)),
                        [t_c, d_w, *free], "p_k" if k else None)
                t_kb = op(DV, lambda e, bank=bank: e.tensor_tensor(
                    KB, bank[:, 0:T].rearrange("p (b a n) -> p b a n", b=G, a=1).to_broadcast([128, G, 4, 64]),
                    rmask[:, 0:4].rearrange("p (a r c) -> p a r c", a=1, c=1).to_broadcast([128, G, 4, 64]),
                    ALU.mult), [m, l_rmask], "d_kb")
                rP.release(i, t_kb)
                for h in range(2):
                    for rp in range(2):
                        c = 8 * (2 * rp + h)
                        t_vb = op(DV, lambda e, l=l, h=h, rp=rp, c=c: e.tensor_scalar(
                            VB[:, :, :, rp, c:c + 8],
                            V3[:, :, 32 * l:32 * l + 32].rearrange("p b (g d) -> p b g d", g=4),
                            rmask[:, 4 + h:5 + h], None, ALU.mult),
                            [t_v3, l_rmask, st["z_vb"], *st.get("vb_free", [])], "d_vb")
                g2 = op(PO, lambda e: e.tensor_tensor(x2[:, :], xT[:, :], xT[:, :], ALU.mult),
                        [t_x, *st.get("x2_free", [])], "g_x2")
                yield
                i, bank, free = rP.take()
                for p in range(NP):
                    m = op(PE, lambda e, p=p, bank=bank: e.matmul(
                        bank[:, T + p:T + p + 1], x2[:, 128 * p:128 * p + 128], mean[:, 0:1],
                        start=True, stop=True), [g2, l_sm, *free])
                m = op(PE, lambda e, l=l, bank=bank: e.matmul(bank[:, 0:T], wqs[:, l, :], xT[:, :],
                                                              start=True, stop=True), [t_x, d_w], "p_q")
                d = op(DV, lambda e, bank=bank: e.tensor_scalar(nt[:, 0, :], bank[:, T:T + NP], EPS, None, ALU.add),
                       [m], "d_ms")
                t_q = op(AC, lambda e, bank=bank: e.copy(Q1, bank[:, 0:T]), [m, d], "a_q")
                rP.release(i, t_q)
                t_inv = rsqrt(nt, inv, d)
                yield
                units = []
                for gg in range(4):
                    ib, bank, free = rS.take()
                    lo = 32 * gg
                    for p in range(NP):
                        for b2 in range(2):
                            b = 2 * p + b2
                            m = op(PE, lambda e, lo=lo, p=p, b=b, b2=b2, bank=bank: e.matmul(
                                bank[64 * b2:64 * b2 + 64, 256 * p:256 * p + 256],
                                Q1[lo:lo + 32, 64 * b:64 * b + 64],
                                KB[lo:lo + 32, b, :, :].rearrange("p r n -> p (r n)"), start=True, stop=True),
                                [t_q, t_kb, *free], "p_s" if b == G - 1 else None)
                    u = dict(bank=bank, ibank=ib)
                    softmax(u, [inv[:, p:p + 1] for p in range(NP)], [t_inv], m)
                    units.append(u)
                    yield
                for u in units:
                    turned(u)
                    yield
                io, obank, free = rP.take()
                for gg in range(4):
                    u = units[gg]
                    for b in range(G):
                        for rp in range(2):
                            n = 256 * (b // 2) + 128 * rp + 64 * (b % 2)
                            m = op(PE, lambda e, gg=gg, b=b, rp=rp, n=n, u=u, obank=obank: e.matmul(
                                obank[32 * gg:32 * gg + 32, 64 * b:64 * b + 64], VB[:, b, gg, rp, :],
                                u["ET"][:, n:n + 64], start=(rp == 0), stop=(rp == 1)),
                                [u["et"], t_vb, *free], "p_pv" if b == G - 1 and rp else None)
                    rE.release(u["iE"], m)
                st["vb_free"] = [m]
                t_ot = copy_out(ot[:, :], obank[:, 0:T], [m], "ot")
                rP.release(io, t_ot)
                yield
                i, bank, free = rP.take()
                m = op(PE, lambda e, l=l, bank=bank: e.matmul(bank[:, 0:T], wos[:, l, :], ot[:, :],
                                                              start=True, stop=True), [t_ot, *free], "p_wo")
                t_x = op(DV, lambda e, bank=bank: e.tensor_tensor(xT[:, :], bank[:, 0:T], xT[:, :], ALU.add),
                         [m], "d_x")
                rP.release(i, t_x)
                yield
            i, bank, free = rP.take()
            for p in range(NP):
                m = op(PE, lambda e, p=p, bank=bank: e.transpose(bank[:, 128 * p:128 * p + 128],
                                                                 xT[:, 128 * p:128 * p + 128], ident[:, :]),
                       [t_x, *free], "p_io" if p == NP - 1 else None)
            st["xT_free"] = [m]
            t_out = copy_out(x2[:, :], bank[:, 0:T], [m, *st.get("x2_free", [])], "xo")
            rP.release(i, t_out)
            r = q.dma(SP, o_r[g], x2[:, :].rearrange("p (k c) -> p k c", k=NP), f"s_o{s}", [t_out])
            st["x2_free"] = [r]
            st["last"] = r
            yield

        def stream(s):
            for g in range(s, NG, NS):
                for _ in group(streams[s], g):
                    yield

        STEPS = 76
        live = [stream(s) for s in range(NS)]
        n = 0
        while live:
            for s, g in list(enumerate(live)):
                if g is None or n < s * STEPS // (2 * NS):
                    continue
                if next(g, "end") == "end":
                    live[s] = None
            n += 1
            if all(g is None for g in live):
                break
        op(SP, lambda e: e.nop(), [st["last"] for st in streams])

        block = ctx.enter_context(nc.Block())

        @block.sync
        def _(e):
            q.play(SP, e)

        @block.tensor
        def _(e):
            q.play(PE, e)

        @block.scalar
        def _(e):
            q.play(AC, e)

        @block.vector
        def _(e):
            q.play(DV, e)

        @block.gpsimd
        def _(e):
            q.play(PO, e)


_INS = ["x", "ctx_2048", "mask_S_fk1", "mask_S_fk0", "L0_xattn_Wq", "L0_xattn_Wk", "L0_xattn_Wv", "L0_xattn_Wo",
        "L0_xattn_bo", "L0_xattn_token_indices_A", "L0_xattn_token_indices_B"] + [
    f"L{l}_xattn_{n}" for l in (1, 2, 3) for n in ("wq", "wk", "wv", "wo", "norm_w")]


def kernel(**inputs):
    import concourse.bacc as _bacc
    from concourse.bass_utils import run_bass_kernel_spmd as _run

    nc = _bacc.Bacc("TRN2", target_bir_lowering=False, num_devices=1)
    arrays, args = {}, {}

    def give(name, a):
        arrays[f"in_{name}"] = a
        args[name] = nc.dram_tensor(f"in_{name}", a.shape, mybir.dt.from_np(a.dtype), kind="ExternalInput").ap()

    for name in _INS:
        give(name, np.ascontiguousarray(inputs[name]))
    rows = np.arange(128)
    give("c_ident", np.eye(128, dtype=np.float32))
    give("c_mean", np.full((128, 128), 1.0 / 128, np.float32))
    give("c_rmask", np.concatenate([rows[:, None] // 8 % 4 == np.arange(4)[None, :],
                                    rows[:, None] // 64 == np.arange(2)[None, :]], 1).astype(np.float32))
    give("c_iota", np.arange(64, dtype=np.float32)[None, :])
    args["out"] = nc.dram_tensor("out_0", (B, S, C), F32, kind="ExternalOutput").ap()
    xattn_kernel(nc, args)
    r = _run(nc, [arrays], core_ids=[0])
    return r.results[0]["out_0"]
```
